# Optimizing a Trainium2 kernel written in Bass

```python
import numpy as np
import jax
import jax.numpy as jnp

def _softmax(x, axis=-1):
    return jax.nn.softmax(x, axis=axis)

def _gelu(x):
    return jax.nn.gelu(x, approximate=True)

def _silu(x):
    return jax.nn.silu(x)

def _sigmoid(x):
    return jax.nn.sigmoid(x)

def _layernorm(x, axis=-1, eps=1e-05):
    m = jnp.mean(x, axis=axis, keepdims=True)
    v = jnp.var(x, axis=axis, keepdims=True)
    return (x - m) / jnp.sqrt(v + eps)

def _scatter_add(tgt, idx, src, axis=0):
    return tgt.at[idx].add(src)

def _segment_sum(src, seg, n):
    return jax.ops.segment_sum(src, seg, n)
kernel_name = 'mk_adj_preln_d1_adj_r2_c4dc38'

def setup_inputs(seed: int=0):
    np.random.seed(seed)
    _w = jnp.asarray

    def _rec_inputs():
        import jax
        import jax.numpy as jnp
        _gk = jax.random.key(seed)
        x = 7.22e-05 + 1 * jax.random.normal(jax.random.fold_in(_gk, 1), (64, 128, 128), jnp.float32)
        _w = (1.0 + jnp.arange(128, dtype=jnp.float32)) ** (-0.5)
        _w = _w / _w.mean()
        _pij = jnp.clip(0.0625 * _w[:, None] * _w[None, :], 0.0, 1.0)
        _a = jax.random.uniform(jax.random.fold_in(_gk, 2), (64, 128, 128)) < _pij
        _af = _a.astype(jnp.float32)
        adj = _af
        _nm = jnp.ones((64, 128), dtype=bool)
        nodemask = jnp.where(_nm, 1.0, 0.0).astype(jnp.float32)
        return (x, adj, nodemask)
    x, adj, nodemask = _rec_inputs()

    def _L0_gnn_setup():
        import jax, jax.numpy as jnp
        import numpy as np
        B, N, D, C, L = (64, 256, 128, 128, 5)
        EDGE_P = 0.02

        def _gru_cell(m, h, w_ih, w_hh, b_ih, b_hh):
            gi = m @ w_ih.T + b_ih
            gh = h @ w_hh.T + b_hh
            i_r, i_z, i_n = jnp.split(gi, 3, axis=-1)
            h_r, h_z, h_n = jnp.split(gh, 3, axis=-1)
            r = jax.nn.sigmoid(i_r + h_r)
            z = jax.nn.sigmoid(i_z + h_z)
            n = jnp.tanh(i_n + r * h_n)
            return (1.0 - z) * n + z * h
        key = jax.random.key(seed)
        ks = jax.random.split(key, 8)
        x = jax.random.normal(ks[0], (B, N, D), dtype=jnp.float32)
        adj = (jax.random.uniform(ks[1], (B, N, N)) < EDGE_P).astype(jnp.float32)
        mask = jnp.ones((B, N), dtype=jnp.float32)
        s = 1.0 / np.sqrt(C).astype(np.float32)
        weight = jax.random.uniform(ks[2], (L, C, C), minval=-s, maxval=s, dtype=jnp.float32)
        w_ih = jax.random.uniform(ks[3], (3 * C, C), minval=-s, maxval=s, dtype=jnp.float32)
        w_hh = jax.random.uniform(ks[4], (3 * C, C), minval=-s, maxval=s, dtype=jnp.float32)
        b_ih = jax.random.uniform(ks[5], (3 * C,), minval=-s, maxval=s, dtype=jnp.float32)
        b_hh = jax.random.uniform(ks[6], (3 * C,), minval=-s, maxval=s, dtype=jnp.float32)
        return dict(x=x, adj=adj, mask=mask, weight=weight, w_ih=w_ih, w_hh=w_hh, b_ih=b_ih, b_hh=b_hh)
    _L0_gnn_all = _L0_gnn_setup()
    _L0_gnn_in = {k: v for k, v in _L0_gnn_all.items() if k in ('weight', 'w_ih', 'w_hh', 'b_ih', 'b_hh')}
    del _L0_gnn_all
    return {'x': x, 'adj': adj, 'nodemask': nodemask, 'L0_gnn_weight': _L0_gnn_in['weight'], 'L0_gnn_w_ih': _L0_gnn_in['w_ih'], 'L0_gnn_w_hh': _L0_gnn_in['w_hh'], 'L0_gnn_b_ih': _L0_gnn_in['b_ih'], 'L0_gnn_b_hh': _L0_gnn_in['b_hh']}

def reference(x, adj, nodemask, L0_gnn_weight, L0_gnn_w_ih, L0_gnn_w_hh, L0_gnn_b_ih, L0_gnn_b_hh):
    import jax
    import jax.numpy as jnp

    def _L0_gnn_ref(x, adj, mask, weight, w_ih, w_hh, b_ih, b_hh):
        import jax, jax.numpy as jnp
        import numpy as np
        B, N, D, C, L = (64, 256, 128, 128, 5)
        EDGE_P = 0.02

        def _gru_cell(m, h, w_ih, w_hh, b_ih, b_hh):
            gi = m @ w_ih.T + b_ih
            gh = h @ w_hh.T + b_hh
            i_r, i_z, i_n = jnp.split(gi, 3, axis=-1)
            h_r, h_z, h_n = jnp.split(gh, 3, axis=-1)
            r = jax.nn.sigmoid(i_r + h_r)
            z = jax.nn.sigmoid(i_z + h_z)
            n = jnp.tanh(i_n + r * h_n)
            return (1.0 - z) * n + z * h
        A = (adj != 0).astype(x.dtype)
        h = x
        for l in range(weight.shape[0]):
            m = jnp.einsum('bnd,de->bne', h, weight[l])
            agg = jnp.einsum('bij,bid->bjd', A, m)
            h = _gru_cell(agg, h, w_ih, w_hh, b_ih, b_hh)
        return h * mask[..., None]
    h = jnp.maximum(_layernorm(x, axis=-1), 0.0)
    x = x + _L0_gnn_ref(h, adj, nodemask, L0_gnn_weight, L0_gnn_w_ih, L0_gnn_w_hh, L0_gnn_b_ih, L0_gnn_b_hh)
    return x

_drawn_inputs = setup_inputs


def setup_inputs(seed=0):
    import zlib

    import numpy as np

    out = dict(_drawn_inputs(seed))
    spreads = {}
    factors = {}
    for name, (base, spread) in spreads.items():
        noise = np.random.default_rng([zlib.crc32(name.encode()), seed]).standard_normal(out[name].shape)
        drawn = base * np.exp(spread * noise) if base else spread * noise
        out[name] = jnp.asarray(drawn.astype(out[name].dtype))
    for name, factor in factors.items():
        out[name] = (out[name] * factor).astype(out[name].dtype)
    return out
```

```python
from contextlib import ExitStack

import concourse.bass as bass
from concourse import mybir

ALU = mybir.AluOpType
ACT = mybir.ActivationFunctionType
F32 = mybir.dt.float32
F32R = mybir.dt.float32r
F16 = mybir.dt.float16

P = 128
TG = 4
TILE = TG * P
SLOTS = 4
GATES = 3
EPS = 1e-05


def gnn_kernel(nc, x, adj, maskT, fold_lhs, w_ihT, w_hhT, bias_ih, bias_hh, ident, out):
    B = x.shape[0]
    L = fold_lhs.shape[1]
    GROUPS = B // (TG * SLOTS)
    UNITS = L * SLOTS
    CG = GATES * P

    x_t = x.rearrange("(t g) n d -> t n g d", g=TG)
    adj_t = adj.rearrange("(t g) i j -> t i g j", g=TG)
    out_t = out.rearrange("(t g) n d -> t n g d", g=TG)

    with ExitStack() as ctx:
        def sb(name, shape, dt=F32):
            return ctx.enter_context(nc.sbuf_tensor(name, shape, dt))

        def bank(name):
            return ctx.enter_context(nc.psum_tensor(name, [P, TILE], F32))

        def sem(name):
            return ctx.enter_context(nc.semaphore(name))

        x_all = sb("x_all", [P, B * P])
        a_all = sb("a_all", [P, B * P], F16)
        adj_in = sb("adj_in", [P, SLOTS * TILE])
        mask_sb = sb("mask_sb", [P, B])
        ident_sb = sb("ident_sb", [P, P])
        fold_in = sb("fold_in", [P, L, P])
        wih_sb = sb("wih_sb", [P, CG])
        whh_sb = sb("whh_sb", [P, CG])
        u_hi = sb("u_hi", [P, CG], F32R)
        u_lo = sb("u_lo", [P, CG], F32R)
        v_all = sb("v_all", [P, L * 2 * CG], F32R)
        v_cur = sb("v_cur", [P, 2 * CG], F32R)
        b_ih = sb("b_ih", [P, GATES])
        b_hh = sb("b_hh", [P, GATES])
        b_sum = sb("b_sum", [P, GATES])
        b_zneg = sb("b_zneg", [P, 1])
        bn = sb("bn", [P, TG, 6])
        mean_var = sb("mean_var", [P, TG, 2])
        var_eps = sb("var_eps", [P, TG])
        eps = sb("eps", [P, TG])
        neg_half = sb("neg_half", [P, TG])
        rstd = sb("rstd", [P, TG])
        neg_mean_rstd = sb("neg_mean_rstd", [P, TG])
        h0 = sb("h0", [P, SLOTS * TILE])
        h = sb("h", [P, SLOTS, TILE])
        h_hi = sb("h_hi", [P, SLOTS, TILE], F32R)
        h_lo = sb("h_lo", [P, SLOTS, TILE], F32R)
        nat_hi = sb("nat_hi", [P, SLOTS, TILE], F16)
        nat_lo = sb("nat_lo", [P, SLOTS, TILE], F16)
        s_hi = sb("s_hi", [P, 2, TILE], F32R)
        s_lo = sb("s_lo", [P, 2, TILE], F32R)
        r = sb("r", [P, TILE])
        z = sb("z", [P, TILE])
        one_z = sb("one_z", [P, TILE])
        rhn = sb("rhn", [P, TILE])
        n = sb("n", [P, TILE])
        zh = sb("zh", [P, TILE])
        zn = sb("zn", [P, TILE])

        ps_r, ps_z, ps_hn, ps_in = bank("ps_r"), bank("ps_z"), bank("ps_hn"), bank("ps_in")
        ps_s, ps_t, ps_t0, ps_v = bank("ps_s"), bank("ps_t"), bank("ps_t0"), bank("ps_v")

        x_loaded = [sem(f"x_loaded{s}") for s in range(SLOTS)]
        adj_loaded = [sem(f"adj_loaded{s}") for s in range(SLOTS)]
        stored = [sem(f"stored{s}") for s in range(SLOTS)]
        w_loaded, wih_loaded = sem("w_loaded"), sem("wih_loaded")
        misc_loaded, ident_loaded = sem("misc_loaded"), sem("ident_loaded")
        v_mm, v_hi_done, v_lo_done = sem("v_mm"), sem("v_hi_done"), sem("v_lo_done")
        u_hi_done, u_lo_done = sem("u_hi_done"), sem("u_lo_done")
        bias_done, vcur_done = sem("bias_done"), sem("vcur_done")
        bn_done, aggr_done, rstd_done = sem("bn_done"), sem("aggr_done"), sem("rstd_done")
        var_done, consts_set = sem("var_done"), sem("consts_set")
        nmr_done, h0_done, a_done = sem("nmr_done"), sem("h0_done"), sem("a_done")
        r_mm, z_mm, in_mm = sem("r_mm"), sem("z_mm"), sem("in_mm")
        s_mm, t_mm, t0_mm = sem("s_mm"), sem("t_mm"), sem("t0_mm")
        h_hi_done, h_lo_done = sem("h_hi_done"), sem("h_lo_done")
        nat_hi_done, nat_lo_done = sem("nat_hi_done"), sem("nat_lo_done")
        s_hi_done, s_lo_done = sem("s_hi_done"), sem("s_lo_done")
        r_done, z_done, one_z_done, n_done = sem("r_done"), sem("z_done"), sem("one_z_done"), sem("n_done")
        rhn_done, npre_done, h_done = sem("rhn_done"), sem("npre_done"), sem("h_done")
        zh_done, zn_done, out_done = sem("zh_done"), sem("zn_done"), sem("out_done")

        def gate(w, k, base=0):
            return w[:, base + k * P:base + (k + 1) * P]

        def graph(tile_ap, q):
            return tile_ap[:, q * P:(q + 1) * P]

        def schedule(eng, first, layer_body, last_body, end):
            first()
            with eng.Fori(0, GROUPS - 1) as g:
                with eng.Fori(0, L - 1) as l:
                    layer_body(g, l, True)
                last_body(g)
            with eng.Fori(0, L - 1) as l:
                layer_body(GROUPS - 1, l, False)
            end(GROUPS - 1)

        block = ctx.enter_context(nc.Block())

        @block.sync
        def _(sp):
            def load_x(t, s):
                sp.dma_start(x_all[:, bass.ds(t * TILE, TILE)].rearrange("p (g d) -> p g d", g=TG),
                             x_t[bass.ds(t, 1)].rearrange("t n g d -> n (t g) d")).then_inc(x_loaded[s], 16)

            def load_adj(t, s):
                sp.dma_start(adj_in[:, s * TILE:(s + 1) * TILE].rearrange("p (g d) -> p g d", g=TG),
                             adj_t[bass.ds(t, 1)].rearrange("t n g d -> n (t g) d")).then_inc(adj_loaded[s], 16)

            load_x(0, 0)
            load_adj(0, 0)
            for s in range(1, SLOTS):
                load_x(s, s)
                load_adj(s, s)
            for s in range(SLOTS):
                sp.wait_ge(a_done, s + 1)
                sp.wait_ge(x_loaded[s], 16)
                load_x(SLOTS + s, s)
                load_adj(SLOTS + s, s)

            def store(g):
                for s in range(SLOTS):
                    sp.wait_ge(out_done, g * SLOTS + s + 1)
                    sp.dma_start(out_t[bass.ds(g * SLOTS + s, 1)].rearrange("t n g d -> n (t g) d"),
                                 x_all[:, bass.ds((g * SLOTS + s) * TILE, TILE)].rearrange(
                                     "p (g d) -> p g d", g=TG)).then_inc(stored[s], 16)

            with sp.Fori(0, GROUPS - 2) as g:
                for s in range(SLOTS):
                    sp.wait_ge(a_done, g * SLOTS + (SLOTS + s + 1))
                    sp.wait_ge(x_loaded[s], g * 16 + 32)
                    load_x(g * SLOTS + (2 * SLOTS + s), s)
                    load_adj(g * SLOTS + (2 * SLOTS + s), s)
                store(g)
            for g in range(GROUPS - 2, GROUPS):
                store(g)
            for s in range(SLOTS):
                sp.wait_ge(stored[s], 16 * GROUPS)

        @block.tensor
        def _(pe):
            def transpose(dst, src):
                for q in range(TG):
                    last = nc.tensor.transpose(graph(dst, q), graph(src, q), ident_sb[:])
                return last

            def three(ps, w_hi, w_lo, m_hi, m_lo, start, stop):
                nc.tensor.matmul(ps[:], w_hi, m_hi, start=start, stop=False)
                nc.tensor.matmul(ps[:], w_hi, m_lo, start=False, stop=False)
                return nc.tensor.matmul(ps[:], w_lo, m_hi, start=False, stop=stop)

            def h_products(K, s):
                pe.wait_ge(h_lo_done, K + 1)
                for k, (ps, last) in enumerate(((ps_r, False), (ps_z, False), (ps_hn, True))):
                    three(ps, gate(u_hi, k), gate(u_lo, k), h_hi[:, s], h_lo[:, s], True, last)

            def banks_free(K):
                pe.wait_ge(one_z_done, K)
                pe.wait_ge(rhn_done, K)

            def s_products(K, s):
                pe.wait_ge(s_lo_done, K + 1)
                par = s % 2
                for k, (ps, ready) in enumerate(((ps_r, r_mm), (ps_z, z_mm), (ps_in, in_mm))):
                    three(ps, gate(v_cur, k), gate(v_cur, k, CG), s_hi[:, par], s_lo[:, par],
                          k == 2, True).then_inc(ready, 1)

            def aggregate(K, tile, s):
                pe.wait_ge(nat_lo_done, K + 1)
                for q in range(TG):
                    a_q = a_all[:, bass.ds((tile + s) * TILE + q * P, P)]
                    nc.tensor.matmul(graph(ps_s, q), graph(nat_hi[:, s], q), a_q, start=True, stop=False)
                    last = nc.tensor.matmul(graph(ps_s, q), graph(nat_lo[:, s], q), a_q, start=False, stop=True)
                last.then_inc(s_mm, 1)

            def step(K, j, tile, layer_starts, next_group, next_unit):
                s = (j + 2) % SLOTS
                banks_free(K)
                h_products(K, s)
                pe.wait_ge(nat_lo_done, K + 2)
                transpose_back(K, j, next_group)
                if next_unit:
                    pe.wait_ge(s_lo_done, K + 1)
                    aggregate(K + 1, tile, (s + 1) % SLOTS)
                pe.wait_ge(n_done, K)
                if layer_starts is not None:
                    pe.wait_ge(vcur_done, layer_starts)
                s_products(K, s)

            def transpose_back(K, j, next_group):
                pe.wait_ge(h_done, K - 1)
                transpose(ps_t, h[:, j]).then_inc(t_mm, 1)
                if next_group is not None:
                    transpose_h0(next_group, j, K + 2)

            def transpose_h0(group, j, before):
                pe.wait_ge(h0_done, group * SLOTS + j + 1)
                if before is not None:
                    pe.wait_ge(h_lo_done, before)
                transpose(ps_t0, h0[:, j * TILE:(j + 1) * TILE]).then_inc(t0_mm, 1)

            def first():
                def fold(l):
                    if l >= 2:
                        pe.wait_ge(v_lo_done, l - 1)
                    nc.tensor.matmul((ps_v if l % 2 == 0 else ps_in)[:, 0:CG], fold_in[:, l], wih_sb[:],
                                     start=True, stop=True).then_inc(v_mm, 1)

                pe.wait_ge(wih_loaded, 32)
                fold(0)
                fold(1)
                pe.wait_ge(ident_loaded, 16)
                for s in range(SLOTS):
                    transpose_h0(0, s, s if s else None)
                    if s == 0:
                        pe.wait_ge(a_done, 1)
                        aggregate(0, 0, 0)
                    if s + 2 < L:
                        fold(s + 2)
                pe.wait_ge(u_lo_done, 1)
                pe.wait_ge(v_lo_done, L)
                for K in range(2):
                    if K >= 1:
                        banks_free(K)
                    h_products(K, K)
                    pe.wait_ge(s_lo_done, K + 1)
                    pe.wait_ge(a_done, K + 2)
                    aggregate(K + 1, 0, K + 1)
                    if K == 0:
                        pe.wait_ge(vcur_done, 1)
                    else:
                        pe.wait_ge(n_done, K)
                    s_products(K, K)

            def layer_body(g, l, more):
                K0 = pe.snap(g * UNITS + l * SLOTS + 2)
                tile = pe.snap(g * SLOTS + l * 0)
                pe.wait_ge(a_done, g * SLOTS + SLOTS)
                for j in range(SLOTS):
                    starts = g * L + l + 2 if j == 2 else None
                    step(K0 + j, j, tile, starts, None, True)

            def last_body(g):
                for j in range(SLOTS):
                    K = g * UNITS + (UNITS - SLOTS + 2 + j)
                    if j:
                        pe.wait_ge(a_done, (g + 1) * SLOTS + j)
                    starts = g * L + (L + 1) if j == 2 else None
                    step(K, j, g * SLOTS + (SLOTS if j else 0), starts, g + 1, True)

            def end(g):
                for j in range(SLOTS):
                    K = g * UNITS + UNITS - SLOTS + 2 + j
                    if j < 2:
                        banks_free(K)
                        h_products(K, j + 2)
                    if j == 0:
                        pe.wait_ge(nat_lo_done, K + 2)
                    else:
                        pe.wait_ge(out_done, g * SLOTS + j)
                    transpose_back(K, j, None)
                    if j == 0:
                        pe.wait_ge(s_lo_done, K + 1)
                        aggregate(K + 1, g * SLOTS, SLOTS - 1)
                    if j < 2:
                        pe.wait_ge(n_done, K)
                        s_products(K, j + 2)

            schedule(pe, first, layer_body, last_body, end)

        @block.scalar
        def _(act):
            def layernorm_apply(count, off, h0_off):
                act.wait_ge(nmr_done, count)
                for q in range(TG):
                    last = nc.scalar.activation(h0[:, bass.ds(h0_off + q * P, P)], x_all[:, bass.ds(off + q * P, P)],
                                                ACT.Relu, bias=neg_mean_rstd[:, q:q + 1], scale=rstd[:, q:q + 1])
                last.then_inc(h0_done, 1)

            def initial_state_high(count, s):
                act.wait_ge(t0_mm, count)
                nc.scalar.copy(h[:, s], ps_t0[:])
                nc.scalar.copy(h_hi[:, s], ps_t0[:]).then_inc(h_hi_done, 1)
                nc.scalar.copy(nat_hi[:, s], h0[:, s * TILE:(s + 1) * TILE]).then_inc(nat_hi_done, 1)

            def s_high(K, par):
                act.wait_ge(s_mm, K + 1)
                nc.scalar.copy(s_hi[:, par], ps_s[:]).then_inc(s_hi_done, 1)

            def gates(K):
                act.wait_ge(r_mm, K + 1)
                nc.scalar.activation(r[:], ps_r[:], ACT.Sigmoid, bias=b_sum[:, 0:1]).then_inc(r_done, 1)
                act.wait_ge(z_mm, K + 1)

            def gate_z(K):
                nc.scalar.activation(z[:], ps_z[:], ACT.Sigmoid, bias=b_sum[:, 1:2]).then_inc(z_done, 1)

            def gate_1z(K):
                nc.scalar.activation(one_z[:], ps_z[:], ACT.Sigmoid, bias=b_zneg[:], scale=-1.0).then_inc(one_z_done, 1)

            def gate_n(K):
                act.wait_ge(npre_done, K + 1)
                nc.scalar.activation(n[:], ps_in[:], ACT.Tanh, bias=b_ih[:, 2:3]).then_inc(n_done, 1)

            def copy_v(K, off):
                act.wait_ge(in_mm, K)
                nc.scalar.copy(v_cur[:], v_all[:, bass.ds(off, 2 * CG)]).then_inc(vcur_done, 1)

            def unit(K, v_off):
                gates(K)
                act.wait_ge(zh_done, K)
                gate_z(K)
                act.wait_ge(zn_done, K)
                gate_1z(K)
                if v_off is not None:
                    copy_v(K + 1, v_off)
                gate_n(K)

            def step(K, j, group, v_off, next_unit, this_unit=True):
                if group is not None:
                    initial_state_high(group * SLOTS + j + 1, j)
                if group is None:
                    act.wait_ge(h_done, K - 1)
                    nc.scalar.copy(h_hi[:, j], h[:, j]).then_inc(h_hi_done, 1)
                    act.wait_ge(t_mm, K - 1)
                    nc.scalar.copy(nat_hi[:, j], ps_t[:]).then_inc(nat_hi_done, 1)
                if next_unit:
                    act.wait_ge(in_mm, K)
                    s_high(K + 1, (j + 3) % 2)
                unit(K, v_off)

            def first():
                act.dma_start(wih_sb[:], w_ihT).then_inc(wih_loaded, 16)
                act.dma_start(fold_in[:], fold_lhs).then_inc(wih_loaded, 16)
                act.dma_start(whh_sb[:], w_hhT).then_inc(w_loaded, 16)
                act.wait_ge(v_mm, 1)
                for l in range(L):
                    act.wait_ge(v_mm, l + 1)
                    nc.scalar.copy(v_all[:, 2 * CG * l:2 * CG * l + CG],
                                   (ps_v if l % 2 == 0 else ps_in)[:, 0:CG]).then_inc(v_hi_done, 1)
                    if l == 0:
                        act.wait_ge(w_loaded, 16)
                        nc.scalar.copy(u_hi[:], whh_sb[:]).then_inc(u_hi_done, 1)
                    if l < SLOTS:
                        layernorm_apply(l + 1, l * TILE, l * TILE)
                        initial_state_high(l + 1, l)
                    if l == 0:
                        s_high(0, 0)
                act.wait_ge(v_lo_done, 1)
                nc.scalar.copy(v_cur[:], v_all[:, 0:2 * CG]).then_inc(vcur_done, 1)
                act.wait_ge(bias_done, 1)
                for K in range(2):
                    s_high(K + 1, (K + 1) % 2)
                    gates(K)
                    if K:
                        act.wait_ge(zh_done, K)
                    gate_z(K)
                    if K:
                        act.wait_ge(zn_done, K)
                    gate_1z(K)
                    gate_n(K)

            def layer_body(g, l, more):
                K0 = act.snap(g * UNITS + l * SLOTS + 2)
                for j in range(SLOTS):
                    step(K0 + j, j, None, (l + 1) * (2 * CG) if j == 1 else None, True)
                    if more and j == 3:
                        layernorm_apply(g * SLOTS + l + (SLOTS + 1), (g * SLOTS + l) * TILE + SLOTS * TILE, l * TILE)

            def last_body(g):
                for j in range(SLOTS):
                    step(g * UNITS + (UNITS - SLOTS + 2 + j), j, g + 1, 0 if j == 1 else None, True)

            def end(g):
                for j in range(2):
                    K = g * UNITS + UNITS - SLOTS + 2 + j
                    if j == 0:
                        act.wait_ge(in_mm, K)
                        s_high(K + 1, (j + 3) % 2)
                    unit(K, None)

            schedule(act, first, layer_body, last_body, end)

        @block.vector
        def _(dve):
            def bn_stats(loaded, off, s_sem):
                dve.wait_ge(s_sem, loaded)
                for q in range(TG):
                    last = nc.vector.bn_stats(bn[:, q], x_all[:, bass.ds(off + q * P, P)])
                last.then_inc(bn_done, 1)

            def bn_aggr():
                for q in range(TG):
                    last = nc.vector.bn_aggr(mean_var[:, q], bn[:, q])
                last.then_inc(aggr_done, 1)

            def negative_mean_rstd(count):
                dve.wait_ge(rstd_done, count)
                nc.vector.scalar_tensor_tensor(out=neg_mean_rstd[:], in0=mean_var[:, :, 0], scalar=-1.0, in1=rstd[:],
                                               op0=ALU.mult, op1=ALU.mult).then_inc(nmr_done, 1)

            def adjacency(loaded, off, in_off, s_sem):
                dve.wait_ge(s_sem, loaded)
                nc.vector.tensor_scalar(a_all[:, bass.ds(off, TILE)], adj_in[:, bass.ds(in_off, TILE)], 0.0, None,
                                        ALU.not_equal).then_inc(a_done, 1)

            def low(dst, whole, high, done):
                nc.vector.tensor_tensor(dst, whole, high, ALU.subtract).then_inc(done, 1)

            def initial_state_low(count, s):
                dve.wait_ge(h_hi_done, count)
                low(h_lo[:, s], ps_t0[:], h_hi[:, s], h_lo_done)
                dve.wait_ge(nat_hi_done, count)
                low(nat_lo[:, s], h0[:, s * TILE:(s + 1) * TILE], nat_hi[:, s], nat_lo_done)

            def s_low(K, par):
                dve.wait_ge(s_hi_done, K + 1)
                low(s_lo[:, par], ps_s[:], s_hi[:, par], s_lo_done)

            def new_state(K, s):
                dve.wait_ge(zn_done, K + 1)
                nc.vector.tensor_tensor(h[:, s], zn[:], zh[:], ALU.add).then_inc(h_done, 1)

            def n_input(K):
                dve.wait_ge(r_done, K + 1)
                nc.vector.scalar_tensor_tensor(out=rhn[:], in0=ps_hn[:], scalar=b_hh[:, 2:3], in1=r[:],
                                               op0=ALU.add, op1=ALU.mult).then_inc(rhn_done, 1)
                dve.wait_ge(in_mm, K + 1)
                dve.wait_ge(rhn_done, K + 1)
                nc.vector.tensor_tensor(ps_in[:], ps_in[:], rhn[:], ALU.add).then_inc(npre_done, 1)

            def final(tile, j, count):
                dve.wait_ge(t_mm, count)
                for q in range(TG):
                    x_q = x_all[:, bass.ds(tile * TILE + (j * TILE + q * P), P)]
                    last = nc.vector.scalar_tensor_tensor(
                        out=x_q, in0=graph(ps_t, q), scalar=mask_sb[:, bass.ds(tile * TG + (j * TG + q), 1)],
                        in1=x_q, op0=ALU.mult, op1=ALU.add)
                last.then_inc(out_done, 1)

            def step(K, j, g, last_layer, next_unit):
                if last_layer:
                    dve.wait_ge(h_hi_done, K + 3)
                    low(h_lo[:, j], ps_t0[:], h_hi[:, j], h_lo_done)
                    final(g * SLOTS, j, K - 1)
                    dve.wait_ge(nat_hi_done, K + 3)
                    low(nat_lo[:, j], h0[:, j * TILE:(j + 1) * TILE], nat_hi[:, j], nat_lo_done)
                else:
                    dve.wait_ge(h_hi_done, K + 3)
                    low(h_lo[:, j], h[:, j], h_hi[:, j], h_lo_done)
                    dve.wait_ge(nat_hi_done, K + 3)
                    low(nat_lo[:, j], ps_t[:], nat_hi[:, j], nat_lo_done)
                if next_unit:
                    s_low(K + 1, (j + 3) % 2)
                new_state(K - 1, (j + 1) % SLOTS)
                n_input(K)

            def first():
                dve.wait_ge(misc_loaded, 48)
                nc.vector.tensor_tensor(b_sum[:], b_ih[:], b_hh[:], ALU.add).then_inc(bias_done, 1)
                dve.wait_ge(bias_done, 1)
                nc.vector.tensor_scalar(b_zneg[:], b_sum[:, 1:2], -1.0, None, ALU.mult).then_inc(bias_done, 1)
                for l in range(L):
                    v_hi = v_all[:, 2 * CG * l:2 * CG * l + CG]
                    v_lo = v_all[:, 2 * CG * l + CG:2 * CG * (l + 1)]
                    if l < SLOTS:
                        bn_stats(16, l * TILE, x_loaded[l])
                        if l:
                            dve.wait_ge(nmr_done, l)
                        dve.wait_ge(bn_done, l + 1)
                        bn_aggr()
                    dve.wait_ge(v_hi_done, l + 1)
                    low(v_lo, (ps_v if l % 2 == 0 else ps_in)[:, 0:CG], v_hi, v_lo_done)
                    if l == 0:
                        dve.wait_ge(u_hi_done, 1)
                        low(u_lo[:], whh_sb[:], u_hi[:], u_lo_done)
                    if l < SLOTS:
                        if l:
                            dve.wait_ge(h0_done, l)
                        negative_mean_rstd(l + 1)
                        adjacency(16, l * TILE, l * TILE, adj_loaded[l])
                        initial_state_low(l + 1, l)
                    if l == 0:
                        s_low(0, 0)
                for K in range(2):
                    s_low(K + 1, (K + 1) % 2)
                    if K:
                        new_state(K - 1, K - 1)
                    n_input(K)

            def layer_body(g, l, more):
                K0 = dve.snap(g * UNITS + l * SLOTS + 2)
                ln_tile = g * SLOTS + l + SLOTS
                if more:
                    ln_off = dve.snap(ln_tile * TILE)
                for j in range(SLOTS):
                    step(K0 + j, j, None, False, True)
                    if more and j == 0:
                        for s in range(1, SLOTS):
                            dve.wait_ge(x_loaded[s], g * 16 + 32)
                        bn_stats(g * 16 + 32, ln_off, x_loaded[0])
                    if more and j == 1:
                        for s in range(1, SLOTS):
                            dve.wait_ge(adj_loaded[s], g * 16 + 32)
                        dve.wait_ge(bn_done, ln_tile + 1)
                        adjacency(g * 16 + 32, ln_off, l * TILE, adj_loaded[0])
                        bn_aggr()
                    if more and j == 2:
                        negative_mean_rstd(ln_tile + 1)

            def last_body(g):
                for j in range(SLOTS):
                    step(g * UNITS + (UNITS - SLOTS + 2 + j), j, g, True, True)

            def end(g):
                for j in range(SLOTS):
                    K = g * UNITS + UNITS - SLOTS + 2 + j
                    final(g * SLOTS, j, K - 1)
                    if j == 0:
                        s_low(K + 1, (j + 3) % 2)
                    if j < 3:
                        new_state(K - 1, (j + 1) % SLOTS)
                    if j < 2:
                        n_input(K)

            schedule(dve, first, layer_body, last_body, end)

        @block.gpsimd
        def _(pool):
            def inv_std(count):
                pool.wait_ge(aggr_done, count)
                nc.gpsimd.tensor_tensor(var_eps[:], mean_var[:, :, 1], eps[:], ALU.add).then_inc(var_done, 1)
                pool.wait_ge(var_done, count)
                nc.gpsimd.tensor_tensor(rstd[:], var_eps[:], neg_half[:], ALU.pow).then_inc(rstd_done, 1)

            def unit(K, s, before=True):
                pool.wait_ge(z_done, K + 1)
                if before:
                    pool.wait_ge(h_done, K)
                nc.gpsimd.tensor_tensor(zh[:], z[:], h[:, s], ALU.mult).then_inc(zh_done, 1)
                pool.wait_ge(n_done, K + 1)
                nc.gpsimd.tensor_tensor(zn[:], one_z[:], n[:], ALU.mult).then_inc(zn_done, 1)

            def first():
                pool.dma_start(b_ih[:], bias_ih).then_inc(misc_loaded, 16)
                pool.dma_start(b_hh[:], bias_hh).then_inc(misc_loaded, 16)
                pool.dma_start(ident_sb[:], ident).then_inc(ident_loaded, 16)
                pool.dma_start(mask_sb[:], maskT).then_inc(misc_loaded, 16)
                nc.gpsimd.memset(eps[:], EPS).then_inc(consts_set, 1)
                nc.gpsimd.memset(neg_half[:], -0.5).then_inc(consts_set, 1)
                pool.wait_ge(consts_set, 2)
                for s in range(SLOTS):
                    if s:
                        pool.wait_ge(h0_done, s)
                    inv_std(s + 1)
                for K in range(2):
                    unit(K, K, K > 0)

            def layer_body(g, l, more):
                K0 = pool.snap(g * UNITS + l * SLOTS + 2)
                for j in range(SLOTS):
                    if more and j == 2:
                        inv_std(g * SLOTS + l + (SLOTS + 1))
                    unit(K0 + j, (j + 2) % SLOTS)

            def last_body(g):
                for j in range(SLOTS):
                    unit(g * UNITS + (UNITS - SLOTS + 2 + j), (j + 2) % SLOTS)

            def end(g):
                for j in range(2):
                    unit(g * UNITS + UNITS - SLOTS + 2 + j, (j + 2) % SLOTS)

            schedule(pool, first, layer_body, last_body, end)


def kernel(x, adj, nodemask, L0_gnn_weight, L0_gnn_w_ih, L0_gnn_w_hh, L0_gnn_b_ih, L0_gnn_b_hh):
    import numpy as np
    import concourse.bacc as bacc
    from concourse.bass_utils import run_bass_kernel_spmd

    nc = bacc.Bacc("TRN2", target_bir_lowering=False, num_devices=1)
    laid_out = {
        "x": np.asarray(x),
        "adj": np.asarray(adj),
        "maskT": np.asarray(nodemask).T,
        "fold_lhs": np.asarray(L0_gnn_weight).transpose(2, 0, 1),
        "w_ihT": np.asarray(L0_gnn_w_ih).T,
        "w_hhT": np.asarray(L0_gnn_w_hh).T,
        "bias_ih": np.asarray(L0_gnn_b_ih).reshape(GATES, P).T,
        "bias_hh": np.asarray(L0_gnn_b_hh).reshape(GATES, P).T,
        "ident": np.eye(P, dtype=np.float32),
    }
    arrays, args = {}, []
    for name, a in laid_out.items():
        a = np.ascontiguousarray(a)
        arrays[f"in_{name}"] = a
        args.append(nc.dram_tensor(f"in_{name}", a.shape, mybir.dt.from_np(a.dtype), kind="ExternalInput").ap())
    out = nc.dram_tensor("out_0", np.asarray(x).shape, F32, kind="ExternalOutput").ap()
    gnn_kernel(nc, *args, out)
    r = run_bass_kernel_spmd(nc, [arrays], core_ids=[0])
    return r.results[0]["out_0"]
```

```python
from contextlib import ExitStack

import concourse.bass as bass
from concourse import mybir

ALU = mybir.AluOpType
ACT = mybir.ActivationFunctionType
F32 = mybir.dt.float32
F32R = mybir.dt.float32r
F16 = mybir.dt.float16

P = 128
TG = 4
TILE = TG * P
SLOTS = 4
GATES = 3
EPS = 1e-05


def gnn_kernel(nc, x, adj, maskT, fold_lhs, w_ihT, w_hhT, bias_ih, bias_hh, ident, out):
    B = x.shape[0]
    L = fold_lhs.shape[1]
    GROUPS = B // (TG * SLOTS)
    UNITS = L * SLOTS
    CG = GATES * P

    x_t = x.rearrange("(t g) n d -> t n g d", g=TG)
    adj_t = adj.rearrange("(t g) i j -> t i g j", g=TG)
    out_t = out.rearrange("(t g) n d -> t n g d", g=TG)

    with ExitStack() as ctx:
        def sb(name, shape, dt=F32):
            return ctx.enter_context(nc.sbuf_tensor(name, shape, dt))

        def bank(name):
            return ctx.enter_context(nc.psum_tensor(name, [P, TILE], F32))

        def sem(name):
            return ctx.enter_context(nc.semaphore(name))

        x_all = sb("x_all", [P, B * P])
        a_all = sb("a_all", [P, B * P], F16)
        adj_in = sb("adj_in", [P, SLOTS * TILE])
        mask_sb = sb("mask_sb", [P, B])
        ident_sb = sb("ident_sb", [P, P])
        fold_in = sb("fold_in", [P, L, P])
        wih_sb = sb("wih_sb", [P, CG])
        whh_sb = sb("whh_sb", [P, CG])
        u_hi = sb("u_hi", [P, CG], F32R)
        u_lo = sb("u_lo", [P, CG], F32R)
        v_all = sb("v_all", [P, L * 2 * CG], F32R)
        v_cur = sb("v_cur", [P, 2 * CG], F32R)
        b_ih = sb("b_ih", [P, GATES])
        b_hh = sb("b_hh", [P, GATES])
        b_sum = sb("b_sum", [P, GATES])
        bn = sb("bn", [P, TG, 6])
        mean_var = sb("mean_var", [P, TG, 2])
        var_eps = sb("var_eps", [P, TG])
        eps = sb("eps", [P, TG])
        neg_half = sb("neg_half", [P, TG])
        rstd = sb("rstd", [P, TG])
        h0 = sb("h0", [P, SLOTS * TILE])
        h = sb("h", [P, SLOTS, TILE])
        h_hi = sb("h_hi", [P, SLOTS, TILE], F32R)
        h_lo = sb("h_lo", [P, SLOTS, TILE], F32R)
        nat_hi = sb("nat_hi", [P, SLOTS, TILE], F16)
        nat_lo = sb("nat_lo", [P, SLOTS, TILE], F16)
        s_hi = sb("s_hi", [P, 2, TILE], F32R)
        s_lo = sb("s_lo", [P, 2, TILE], F32R)
        r = sb("r", [P, TILE])
        z = sb("z", [P, 2, TILE])
        rhn = sb("rhn", [P, TILE])
        n = sb("n", [P, 2, TILE])
        diff = sb("diff", [P, TILE])
        zdiff = sb("zdiff", [P, TILE])

        ps_r, ps_z, ps_hn, ps_in = bank("ps_r"), bank("ps_z"), bank("ps_hn"), bank("ps_in")
        ps_s, ps_t, ps_t0, ps_v = bank("ps_s"), bank("ps_t"), bank("ps_t0"), bank("ps_v")

        x_loaded = [sem(f"x_loaded{s}") for s in range(SLOTS)]
        adj_loaded = [sem(f"adj_loaded{s}") for s in range(SLOTS)]
        stored = [sem(f"stored{s}") for s in range(SLOTS)]
        w_loaded, wih_loaded = sem("w_loaded"), sem("wih_loaded")
        misc_loaded, ident_loaded = sem("misc_loaded"), sem("ident_loaded")
        v_mm, v_hi_done, v_lo_done = sem("v_mm"), sem("v_hi_done"), sem("v_lo_done")
        u_hi_done, u_lo_done = sem("u_hi_done"), sem("u_lo_done")
        bias_done, vcur_done = sem("bias_done"), sem("vcur_done")
        bn_done, aggr_done, rstd_done = sem("bn_done"), sem("aggr_done"), sem("rstd_done")
        var_done, consts_set = sem("var_done"), sem("consts_set")
        h0_done, a_done = sem("h0_done"), sem("a_done")
        r_mm, z_mm, in_mm = sem("r_mm"), sem("z_mm"), sem("in_mm")
        s_mm, t_mm, t0_mm = sem("s_mm"), sem("t_mm"), sem("t0_mm")
        h_hi_done, h_lo_done = sem("h_hi_done"), sem("h_lo_done")
        nat_hi_done, nat_lo_done = sem("nat_hi_done"), sem("nat_lo_done")
        s_hi_done, s_lo_done = sem("s_hi_done"), sem("s_lo_done")
        r_done, z_done, n_done = sem("r_done"), sem("z_done"), sem("n_done")
        rhn_done, npre_done, h_done = sem("rhn_done"), sem("npre_done"), sem("h_done")
        diff_done, zdiff_done, out_done = sem("diff_done"), sem("zdiff_done"), sem("out_done")

        def gate(w, k, base=0):
            return w[:, base + k * P:base + (k + 1) * P]

        def graph(tile_ap, q):
            return tile_ap[:, q * P:(q + 1) * P]

        def schedule(eng, first, layer_body, last_body, end):
            first()
            with eng.Fori(0, GROUPS - 1) as g:
                with eng.Fori(0, L - 1) as l:
                    layer_body(g, l, True)
                last_body(g)
            with eng.Fori(0, L - 1) as l:
                layer_body(GROUPS - 1, l, False)
            end(GROUPS - 1)

        block = ctx.enter_context(nc.Block())

        @block.sync
        def _(sp):
            def load_x(t, s):
                sp.dma_start(x_all[:, bass.ds(t * TILE, TILE)].rearrange("p (g d) -> p g d", g=TG),
                             x_t[bass.ds(t, 1)].rearrange("t n g d -> n (t g) d")).then_inc(x_loaded[s], 16)

            def load_adj(t, s):
                sp.dma_start(adj_in[:, s * TILE:(s + 1) * TILE].rearrange("p (g d) -> p g d", g=TG),
                             adj_t[bass.ds(t, 1)].rearrange("t n g d -> n (t g) d")).then_inc(adj_loaded[s], 16)

            load_x(0, 0)
            load_adj(0, 0)
            for s in range(1, SLOTS):
                load_x(s, s)
                load_adj(s, s)
            for s in range(SLOTS):
                sp.wait_ge(a_done, s + 1)
                sp.wait_ge(x_loaded[s], 16)
                load_x(SLOTS + s, s)
                load_adj(SLOTS + s, s)

            def store(g):
                for s in range(SLOTS):
                    sp.wait_ge(out_done, g * SLOTS + s + 1)
                    sp.dma_start(out_t[bass.ds(g * SLOTS + s, 1)].rearrange("t n g d -> n (t g) d"),
                                 x_all[:, bass.ds((g * SLOTS + s) * TILE, TILE)].rearrange(
                                     "p (g d) -> p g d", g=TG)).then_inc(stored[s], 16)

            with sp.Fori(0, GROUPS - 2) as g:
                for s in range(SLOTS):
                    sp.wait_ge(a_done, g * SLOTS + (SLOTS + s + 1))
                    sp.wait_ge(x_loaded[s], g * 16 + 32)
                    load_x(g * SLOTS + (2 * SLOTS + s), s)
                    load_adj(g * SLOTS + (2 * SLOTS + s), s)
                store(g)
            for g in range(GROUPS - 2, GROUPS):
                store(g)
            for s in range(SLOTS):
                sp.wait_ge(stored[s], 16 * GROUPS)

        @block.tensor
        def _(pe):
            def transpose(dst, src):
                for q in range(TG):
                    last = nc.tensor.transpose(graph(dst, q), graph(src, q), ident_sb[:])
                return last

            def three(ps, w_hi, w_lo, m_hi, m_lo, start, stop):
                nc.tensor.matmul(ps[:], w_hi, m_hi, start=start, stop=False)
                nc.tensor.matmul(ps[:], w_hi, m_lo, start=False, stop=False)
                return nc.tensor.matmul(ps[:], w_lo, m_hi, start=False, stop=stop)

            def h_products(K, s, first_unit=False):
                pe.wait_ge(h_lo_done, K + 1)
                if not first_unit:
                    pe.wait_ge(r_done, K)
                three(ps_r, gate(u_hi, 0), gate(u_lo, 0), h_hi[:, s], h_lo[:, s], True, False)
                if not first_unit:
                    pe.wait_ge(z_done, K)
                three(ps_z, gate(u_hi, 1), gate(u_lo, 1), h_hi[:, s], h_lo[:, s], True, False)
                if not first_unit:
                    pe.wait_ge(rhn_done, K)
                three(ps_hn, gate(u_hi, 2), gate(u_lo, 2), h_hi[:, s], h_lo[:, s], True, True)

            def s_products(K, s):
                pe.wait_ge(s_lo_done, K + 1)
                par = s % 2
                for k, (ps, ready) in enumerate(((ps_r, r_mm), (ps_z, z_mm), (ps_in, in_mm))):
                    three(ps, gate(v_cur, k), gate(v_cur, k, CG), s_hi[:, par], s_lo[:, par],
                          k == 2, True).then_inc(ready, 1)

            def aggregate(K, tile, s):
                pe.wait_ge(nat_lo_done, K + 1)
                for q in range(TG):
                    a_q = a_all[:, bass.ds((tile + s) * TILE + q * P, P)]
                    nc.tensor.matmul(graph(ps_s, q), graph(nat_hi[:, s], q), a_q, start=True, stop=False)
                    last = nc.tensor.matmul(graph(ps_s, q), graph(nat_lo[:, s], q), a_q, start=False, stop=True)
                last.then_inc(s_mm, 1)

            def step(K, j, tile, layer_starts, next_group, next_unit):
                s = (j + 2) % SLOTS
                h_products(K, s)
                pe.wait_ge(nat_lo_done, K + 2)
                transpose_back(K, j, next_group)
                if next_unit:
                    pe.wait_ge(s_lo_done, K + 1)
                    aggregate(K + 1, tile, (s + 1) % SLOTS)
                pe.wait_ge(n_done, K)
                if layer_starts is not None:
                    pe.wait_ge(vcur_done, layer_starts)
                s_products(K, s)

            def transpose_back(K, j, next_group):
                pe.wait_ge(h_done, K - 1)
                transpose(ps_t, h[:, j]).then_inc(t_mm, 1)
                if next_group is not None:
                    transpose_h0(next_group, j, K + 2)

            def transpose_h0(group, j, before):
                pe.wait_ge(h0_done, group * SLOTS + j + 1)
                if before is not None:
                    pe.wait_ge(h_lo_done, before)
                transpose(ps_t0, h0[:, j * TILE:(j + 1) * TILE]).then_inc(t0_mm, 1)

            def first():
                def fold(l):
                    if l >= 2:
                        pe.wait_ge(v_lo_done, l - 1)
                    nc.tensor.matmul((ps_v if l % 2 == 0 else ps_in)[:, 0:CG], fold_in[:, l], wih_sb[:],
                                     start=True, stop=True).then_inc(v_mm, 1)

                pe.wait_ge(wih_loaded, 32)
                fold(0)
                fold(1)
                pe.wait_ge(ident_loaded, 16)
                for s in range(SLOTS):
                    transpose_h0(0, s, s if s else None)
                    if s == 0:
                        pe.wait_ge(a_done, 1)
                        aggregate(0, 0, 0)
                    if s + 2 < L:
                        fold(s + 2)
                pe.wait_ge(u_lo_done, 1)
                pe.wait_ge(v_lo_done, L)
                for K in range(2):
                    h_products(K, K, K == 0)
                    pe.wait_ge(s_lo_done, K + 1)
                    pe.wait_ge(a_done, K + 2)
                    aggregate(K + 1, 0, K + 1)
                    if K == 0:
                        pe.wait_ge(vcur_done, 1)
                    else:
                        pe.wait_ge(n_done, K)
                    s_products(K, K)

            def layer_body(g, l, more):
                K0 = pe.snap(g * UNITS + l * SLOTS + 2)
                tile = pe.snap(g * SLOTS + l * 0)
                pe.wait_ge(a_done, g * SLOTS + SLOTS)
                for j in range(SLOTS):
                    starts = g * L + l + 2 if j == 2 else None
                    step(K0 + j, j, tile, starts, None, True)

            def last_body(g):
                for j in range(SLOTS):
                    K = g * UNITS + (UNITS - SLOTS + 2 + j)
                    if j:
                        pe.wait_ge(a_done, (g + 1) * SLOTS + j)
                    starts = g * L + (L + 1) if j == 2 else None
                    step(K, j, g * SLOTS + (SLOTS if j else 0), starts, g + 1, True)

            def end(g):
                for j in range(SLOTS):
                    K = g * UNITS + UNITS - SLOTS + 2 + j
                    if j < 2:
                        h_products(K, j + 2)
                    if j == 0:
                        pe.wait_ge(nat_lo_done, K + 2)
                    else:
                        pe.wait_ge(out_done, g * SLOTS + j)
                    transpose_back(K, j, None)
                    if j == 0:
                        pe.wait_ge(s_lo_done, K + 1)
                        aggregate(K + 1, g * SLOTS, SLOTS - 1)
                    if j < 2:
                        pe.wait_ge(n_done, K)
                        s_products(K, j + 2)

            schedule(pe, first, layer_body, last_body, end)

        @block.scalar
        def _(act):
            def initial_state_high(count, s):
                act.wait_ge(t0_mm, count)
                nc.scalar.activation(h[:, s], ps_t0[:], ACT.Relu)
                nc.scalar.activation(h_hi[:, s], ps_t0[:], ACT.Relu).then_inc(h_hi_done, 1)
                nc.scalar.activation(nat_hi[:, s], h0[:, s * TILE:(s + 1) * TILE], ACT.Relu).then_inc(nat_hi_done, 1)

            def s_high(K, par):
                act.wait_ge(s_mm, K + 1)
                nc.scalar.copy(s_hi[:, par], ps_s[:]).then_inc(s_hi_done, 1)

            def gate_r(K):
                act.wait_ge(r_mm, K + 1)
                nc.scalar.activation(r[:], ps_r[:], ACT.Sigmoid, bias=b_sum[:, 0:1]).then_inc(r_done, 1)

            def gate_z(K, par, prologue=False):
                act.wait_ge(z_mm, K + 1)
                if not prologue:
                    act.wait_ge(zdiff_done, K - 1)
                nc.scalar.activation(z[:, par], ps_z[:], ACT.Sigmoid, bias=b_sum[:, 1:2]).then_inc(z_done, 1)

            def gate_n(K, par, prologue=False):
                act.wait_ge(npre_done, K + 1)
                if not prologue:
                    act.wait_ge(h_done, K - 1)
                nc.scalar.activation(n[:, par], ps_in[:], ACT.Tanh, bias=b_ih[:, 2:3]).then_inc(n_done, 1)

            def copy_v(K, off):
                act.wait_ge(in_mm, K)
                nc.scalar.copy(v_cur[:], v_all[:, bass.ds(off, 2 * CG)]).then_inc(vcur_done, 1)

            def unit(K, par, v_off):
                gate_r(K)
                gate_z(K, par)
                if v_off is not None:
                    copy_v(K + 1, v_off)
                gate_n(K, par)

            def step(K, j, group, v_off, next_unit):
                if group is not None:
                    initial_state_high(group * SLOTS + j + 1, j)
                if group is None:
                    act.wait_ge(h_done, K - 1)
                    nc.scalar.copy(h_hi[:, j], h[:, j]).then_inc(h_hi_done, 1)
                    act.wait_ge(t_mm, K - 1)
                    nc.scalar.copy(nat_hi[:, j], ps_t[:]).then_inc(nat_hi_done, 1)
                if next_unit:
                    act.wait_ge(in_mm, K)
                    s_high(K + 1, (j + 3) % 2)
                unit(K, j % 2, v_off)

            def first():
                act.dma_start(wih_sb[:], w_ihT).then_inc(wih_loaded, 16)
                act.dma_start(fold_in[:], fold_lhs).then_inc(wih_loaded, 16)
                act.dma_start(whh_sb[:], w_hhT).then_inc(w_loaded, 16)
                act.wait_ge(v_mm, 1)
                for l in range(L):
                    act.wait_ge(v_mm, l + 1)
                    nc.scalar.copy(v_all[:, 2 * CG * l:2 * CG * l + CG],
                                   (ps_v if l % 2 == 0 else ps_in)[:, 0:CG]).then_inc(v_hi_done, 1)
                    if l == 0:
                        act.wait_ge(w_loaded, 16)
                        nc.scalar.copy(u_hi[:], whh_sb[:]).then_inc(u_hi_done, 1)
                    if l < SLOTS:
                        initial_state_high(l + 1, l)
                    if l == 0:
                        s_high(0, 0)
                act.wait_ge(v_lo_done, 1)
                nc.scalar.copy(v_cur[:], v_all[:, 0:2 * CG]).then_inc(vcur_done, 1)
                act.wait_ge(bias_done, 1)
                for K in range(2):
                    s_high(K + 1, (K + 1) % 2)
                    gate_r(K)
                    gate_z(K, K, True)
                    gate_n(K, K, True)

            def layer_body(g, l, more):
                K0 = act.snap(g * UNITS + l * SLOTS + 2)
                for j in range(SLOTS):
                    step(K0 + j, j, None, (l + 1) * (2 * CG) if j == 1 else None, True)

            def last_body(g):
                for j in range(SLOTS):
                    step(g * UNITS + (UNITS - SLOTS + 2 + j), j, g + 1, 0 if j == 1 else None, True)

            def end(g):
                for j in range(2):
                    K = g * UNITS + UNITS - SLOTS + 2 + j
                    if j == 0:
                        act.wait_ge(in_mm, K)
                        s_high(K + 1, (j + 3) % 2)
                    unit(K, j % 2, None)

            schedule(act, first, layer_body, last_body, end)

        @block.vector
        def _(dve):
            def bn_stats(loaded, off, s_sem):
                dve.wait_ge(s_sem, loaded)
                for q in range(TG):
                    last = nc.vector.bn_stats(bn[:, q], x_all[:, bass.ds(off + q * P, P)])
                last.then_inc(bn_done, 1)

            def bn_aggr():
                for q in range(TG):
                    last = nc.vector.bn_aggr(mean_var[:, q], bn[:, q])
                last.then_inc(aggr_done, 1)

            def layernorm(count, off, h0_off):
                dve.wait_ge(rstd_done, count)
                for q in range(TG):
                    last = nc.vector.tensor_scalar(h0[:, bass.ds(h0_off + q * P, P)], x_all[:, bass.ds(off + q * P, P)],
                                                   mean_var[:, q, 0:1], rstd[:, q:q + 1], ALU.subtract, ALU.mult)
                last.then_inc(h0_done, 1)

            def adjacency(loaded, off, in_off, s_sem):
                dve.wait_ge(s_sem, loaded)
                nc.vector.tensor_scalar(a_all[:, bass.ds(off, TILE)], adj_in[:, bass.ds(in_off, TILE)], 0.0, None,
                                        ALU.not_equal).then_inc(a_done, 1)

            def low(dst, whole, high, done):
                nc.vector.tensor_tensor(dst, whole, high, ALU.subtract).then_inc(done, 1)

            def initial_state_low(count, s):
                dve.wait_ge(h_hi_done, count)
                low(h_lo[:, s], h[:, s], h_hi[:, s], h_lo_done)
                initial_natural_low(count, s)

            def initial_natural_low(count, s):
                dve.wait_ge(nat_hi_done, count)
                nc.vector.scalar_tensor_tensor(out=nat_lo[:, s], in0=h0[:, s * TILE:(s + 1) * TILE], scalar=0.0,
                                               in1=nat_hi[:, s], op0=ALU.max, op1=ALU.subtract).then_inc(nat_lo_done, 1)

            def s_low(K, par):
                dve.wait_ge(s_hi_done, K + 1)
                low(s_lo[:, par], ps_s[:], s_hi[:, par], s_lo_done)

            def new_state(K, s):
                dve.wait_ge(zdiff_done, K + 1)
                nc.vector.tensor_tensor(h[:, s], n[:, s % 2], zdiff[:], ALU.add).then_inc(h_done, 1)

            def r_times_hn(K):
                dve.wait_ge(r_done, K + 1)
                nc.vector.scalar_tensor_tensor(out=rhn[:], in0=ps_hn[:], scalar=b_hh[:, 2:3], in1=r[:],
                                               op0=ALU.add, op1=ALU.mult).then_inc(rhn_done, 1)

            def n_input(K):
                dve.wait_ge(in_mm, K + 1)
                dve.wait_ge(rhn_done, K + 1)
                nc.vector.tensor_tensor(ps_in[:], ps_in[:], rhn[:], ALU.add).then_inc(npre_done, 1)

            def final(tile, j, count):
                dve.wait_ge(t_mm, count)
                for q in range(TG):
                    x_q = x_all[:, bass.ds(tile * TILE + (j * TILE + q * P), P)]
                    last = nc.vector.scalar_tensor_tensor(
                        out=x_q, in0=graph(ps_t, q), scalar=mask_sb[:, bass.ds(tile * TG + (j * TG + q), 1)],
                        in1=x_q, op0=ALU.mult, op1=ALU.add)
                last.then_inc(out_done, 1)

            def step(K, j, g, last_layer, next_unit):
                dve.wait_ge(h_hi_done, K + 3)
                low(h_lo[:, j], h[:, j], h_hi[:, j], h_lo_done)
                if last_layer:
                    final(g * SLOTS, j, K - 1)
                    initial_natural_low(K + 3, j)
                else:
                    dve.wait_ge(nat_hi_done, K + 3)
                    low(nat_lo[:, j], ps_t[:], nat_hi[:, j], nat_lo_done)
                if next_unit:
                    s_low(K + 1, (j + 3) % 2)
                r_times_hn(K)
                new_state(K - 1, (j + 1) % SLOTS)
                n_input(K)

            def first():
                dve.wait_ge(misc_loaded, 48)
                nc.vector.tensor_tensor(b_sum[:], b_ih[:], b_hh[:], ALU.add).then_inc(bias_done, 1)
                for l in range(L):
                    v_hi = v_all[:, 2 * CG * l:2 * CG * l + CG]
                    v_lo = v_all[:, 2 * CG * l + CG:2 * CG * (l + 1)]
                    if l < SLOTS:
                        bn_stats(16, l * TILE, x_loaded[l])
                        dve.wait_ge(bn_done, l + 1)
                        bn_aggr()
                    dve.wait_ge(v_hi_done, l + 1)
                    low(v_lo, (ps_v if l % 2 == 0 else ps_in)[:, 0:CG], v_hi, v_lo_done)
                    if l == 0:
                        dve.wait_ge(u_hi_done, 1)
                        low(u_lo[:], whh_sb[:], u_hi[:], u_lo_done)
                    if l < SLOTS:
                        layernorm(l + 1, l * TILE, l * TILE)
                        adjacency(16, l * TILE, l * TILE, adj_loaded[l])
                        initial_state_low(l + 1, l)
                    if l == 0:
                        s_low(0, 0)
                for K in range(2):
                    s_low(K + 1, (K + 1) % 2)
                    r_times_hn(K)
                    if K:
                        new_state(K - 1, K - 1)
                    n_input(K)

            def layer_body(g, l, more):
                K0 = dve.snap(g * UNITS + l * SLOTS + 2)
                ln_tile = g * SLOTS + l + SLOTS
                if more:
                    ln_off = dve.snap(ln_tile * TILE)
                for j in range(SLOTS):
                    step(K0 + j, j, None, False, True)
                    if more and j == 0:
                        for s in range(1, SLOTS):
                            dve.wait_ge(x_loaded[s], g * 16 + 32)
                        bn_stats(g * 16 + 32, ln_off, x_loaded[0])
                    if more and j == 1:
                        for s in range(1, SLOTS):
                            dve.wait_ge(adj_loaded[s], g * 16 + 32)
                        dve.wait_ge(bn_done, ln_tile + 1)
                        adjacency(g * 16 + 32, ln_off, l * TILE, adj_loaded[0])
                        bn_aggr()
                    if more and j == 3:
                        layernorm(ln_tile + 1, ln_off, l * TILE)

            def last_body(g):
                for j in range(SLOTS):
                    step(g * UNITS + (UNITS - SLOTS + 2 + j), j, g, True, True)

            def end(g):
                for j in range(SLOTS):
                    K = g * UNITS + UNITS - SLOTS + 2 + j
                    final(g * SLOTS, j, K - 1)
                    if j == 0:
                        s_low(K + 1, (j + 3) % 2)
                    if j < 2:
                        r_times_hn(K)
                    if j < 3:
                        new_state(K - 1, (j + 1) % SLOTS)
                    if j < 2:
                        n_input(K)

            schedule(dve, first, layer_body, last_body, end)

        @block.gpsimd
        def _(pool):
            def inv_std(count):
                pool.wait_ge(aggr_done, count)
                nc.gpsimd.tensor_tensor(var_eps[:], mean_var[:, :, 1], eps[:], ALU.add).then_inc(var_done, 1)
                pool.wait_ge(var_done, count)
                nc.gpsimd.tensor_tensor(rstd[:], var_eps[:], neg_half[:], ALU.pow).then_inc(rstd_done, 1)

            def unit(K, s, before=True):
                pool.wait_ge(n_done, K + 1)
                nc.gpsimd.tensor_tensor(diff[:], h[:, s], n[:, s % 2], ALU.subtract).then_inc(diff_done, 1)
                if before:
                    pool.wait_ge(h_done, K)
                pool.wait_ge(diff_done, K + 1)
                nc.gpsimd.tensor_tensor(zdiff[:], z[:, s % 2], diff[:], ALU.mult).then_inc(zdiff_done, 1)

            def first():
                pool.dma_start(b_ih[:], bias_ih).then_inc(misc_loaded, 16)
                pool.dma_start(b_hh[:], bias_hh).then_inc(misc_loaded, 16)
                pool.dma_start(ident_sb[:], ident).then_inc(ident_loaded, 16)
                pool.dma_start(mask_sb[:], maskT).then_inc(misc_loaded, 16)
                nc.gpsimd.memset(eps[:], EPS).then_inc(consts_set, 1)
                nc.gpsimd.memset(neg_half[:], -0.5).then_inc(consts_set, 1)
                pool.wait_ge(consts_set, 2)
                for s in range(SLOTS):
                    if s:
                        pool.wait_ge(h0_done, s)
                    inv_std(s + 1)
                for K in range(2):
                    unit(K, K, K > 0)

            def layer_body(g, l, more):
                K0 = pool.snap(g * UNITS + l * SLOTS + 2)
                for j in range(SLOTS):
                    if more and j == 2:
                        inv_std(g * SLOTS + l + (SLOTS + 1))
                    unit(K0 + j, (j + 2) % SLOTS)

            def last_body(g):
                for j in range(SLOTS):
                    unit(g * UNITS + (UNITS - SLOTS + 2 + j), (j + 2) % SLOTS)

            def end(g):
                for j in range(2):
                    unit(g * UNITS + UNITS - SLOTS + 2 + j, (j + 2) % SLOTS)

            schedule(pool, first, layer_body, last_body, end)


def kernel(x, adj, nodemask, L0_gnn_weight, L0_gnn_w_ih, L0_gnn_w_hh, L0_gnn_b_ih, L0_gnn_b_hh):
    import numpy as np
    import concourse.bacc as bacc
    from concourse.bass_utils import run_bass_kernel_spmd

    nc = bacc.Bacc("TRN2", target_bir_lowering=False, num_devices=1)
    laid_out = {
        "x": np.asarray(x),
        "adj": np.asarray(adj),
        "maskT": np.asarray(nodemask).T,
        "fold_lhs": np.asarray(L0_gnn_weight).transpose(2, 0, 1),
        "w_ihT": np.asarray(L0_gnn_w_ih).T,
        "w_hhT": np.asarray(L0_gnn_w_hh).T,
        "bias_ih": np.asarray(L0_gnn_b_ih).reshape(GATES, P).T,
        "bias_hh": np.asarray(L0_gnn_b_hh).reshape(GATES, P).T,
        "ident": np.eye(P, dtype=np.float32),
    }
    arrays, args = {}, []
    for name, a in laid_out.items():
        a = np.ascontiguousarray(a)
        arrays[f"in_{name}"] = a
        args.append(nc.dram_tensor(f"in_{name}", a.shape, mybir.dt.from_np(a.dtype), kind="ExternalInput").ap())
    out = nc.dram_tensor("out_0", np.asarray(x).shape, F32, kind="ExternalOutput").ap()
    gnn_kernel(nc, *args, out)
    r = run_bass_kernel_spmd(nc, [arrays], core_ids=[0])
    return r.results[0]["out_0"]
```

```python
from contextlib import ExitStack

import concourse.bass as bass
from concourse import mybir

ALU = mybir.AluOpType
ACT = mybir.ActivationFunctionType
F32 = mybir.dt.float32
F32R = mybir.dt.float32r
F16 = mybir.dt.float16

P = 128
TG = 4
TILE = TG * P
SLOTS = 4
GATES = 3
EPS = 1e-05


def gnn_kernel(nc, x, adj, maskT, fold_lhs, w_ihT, w_hhT, bias_ih, bias_hh, ident, out):
    B = x.shape[0]
    L = fold_lhs.shape[1]
    GROUPS = B // (TG * SLOTS)
    UNITS = L * SLOTS
    CG = GATES * P

    x_t = x.rearrange("(t g) n d -> t n g d", g=TG)
    adj_t = adj.rearrange("(t g) i j -> t i g j", g=TG)
    out_t = out.rearrange("(t g) n d -> t n g d", g=TG)

    with ExitStack() as ctx:
        def sb(name, shape, dt=F32):
            return ctx.enter_context(nc.sbuf_tensor(name, shape, dt))

        def bank(name):
            return ctx.enter_context(nc.psum_tensor(name, [P, TILE], F32))

        def sem(name):
            return ctx.enter_context(nc.semaphore(name))

        x_all = sb("x_all", [P, B * P])
        adj_in = sb("adj_in", [P, SLOTS, TILE])
        mask_sb = sb("mask_sb", [P, B])
        ident_sb = sb("ident_sb", [P, P])
        fold_in = sb("fold_in", [P, L, P])
        wih_sb = sb("wih_sb", [P, CG])
        whh_sb = sb("whh_sb", [P, CG])
        v_whole = sb("v_whole", [P, CG])
        table_warm = sb("table_warm", [P, 1])
        u_hi = sb("u_hi", [P, CG], F32R)
        u_lo = sb("u_lo", [P, CG], F32R)
        v_all = sb("v_all", [P, L * 2 * CG], F32R)
        v_cur = sb("v_cur", [P, 2 * CG], F32R)
        b_ih = sb("b_ih", [P, GATES])
        b_hh = sb("b_hh", [P, GATES])
        b_sum = sb("b_sum", [P, GATES])
        bn = sb("bn", [P, TG, 6])
        mean_var = sb("mean_var", [P, 2, TG, 2])
        var_eps = sb("var_eps", [P, 2, TG])
        eps = sb("eps", [P, TG])
        neg_half = sb("neg_half", [P, TG])
        rstd = sb("rstd", [P, 2, TG])
        h0 = sb("h0", [P, SLOTS * TILE])
        a = sb("a", [P, SLOTS, TILE], F16)
        h = sb("h", [P, SLOTS, TILE])
        h_hi = sb("h_hi", [P, SLOTS, TILE], F32R)
        h_lo = sb("h_lo", [P, SLOTS, TILE], F32R)
        nat_hi = sb("nat_hi", [P, SLOTS, TILE], F16)
        nat_lo = sb("nat_lo", [P, SLOTS, TILE], F16)
        s_hi = sb("s_hi", [P, 2, TILE], F32R)
        s_lo = sb("s_lo", [P, 2, TILE], F32R)
        r = sb("r", [P, TILE])
        z = sb("z", [P, 2, TILE])
        rhn = sb("rhn", [P, TILE])
        n = sb("n", [P, 2, TILE])
        diff = sb("diff", [P, TILE])
        zdiff = sb("zdiff", [P, TILE])

        ps_r, ps_z, ps_hn, ps_in = bank("ps_r"), bank("ps_z"), bank("ps_hn"), bank("ps_in")
        ps_s, ps_t, ps_t0, ps_v = bank("ps_s"), bank("ps_t"), bank("ps_t0"), bank("ps_v")

        x_loaded = [sem(f"x_loaded{s}") for s in range(SLOTS)]
        adj_loaded = [sem(f"adj_loaded{s}") for s in range(SLOTS)]
        stored = [sem(f"stored{s}") for s in range(SLOTS)]
        w_loaded, wih_loaded = sem("w_loaded"), sem("wih_loaded")
        misc_loaded, ident_loaded = sem("misc_loaded"), sem("ident_loaded")
        v_mm, v_hi_done, v_lo_done = sem("v_mm"), sem("v_hi_done"), sem("v_lo_done")
        u_hi_done, u_lo_done = sem("u_hi_done"), sem("u_lo_done")
        bias_done, vcur_done = sem("bias_done"), sem("vcur_done")
        bn_done, aggr_done, rstd_done = sem("bn_done"), sem("aggr_done"), sem("rstd_done")
        var_done, consts_set = sem("var_done"), sem("consts_set")
        h0_done, a_done = sem("h0_done"), sem("a_done")
        r_mm, z_mm, in_mm = sem("r_mm"), sem("z_mm"), sem("in_mm")
        s_mm, t_mm, t0_mm = sem("s_mm"), sem("t_mm"), sem("t0_mm")
        h_hi_done, h_lo_done = sem("h_hi_done"), sem("h_lo_done")
        nat_hi_done, nat_lo_done = sem("nat_hi_done"), sem("nat_lo_done")
        s_hi_done, s_lo_done = sem("s_hi_done"), sem("s_lo_done")
        r_done, z_done, n_done = sem("r_done"), sem("z_done"), sem("n_done")
        rhn_done, npre_done, h_done = sem("rhn_done"), sem("npre_done"), sem("h_done")
        diff_done, zdiff_done, out_done = sem("diff_done"), sem("zdiff_done"), sem("out_done")

        ps_back = (ps_t, ps_v)

        def gate(w, k, base=0):
            return w[:, base + k * P:base + (k + 1) * P]

        def graph(tile_ap, q):
            return tile_ap[:, q * P:(q + 1) * P]

        def schedule(eng, first, layer_body, last_body, end):
            first()
            with eng.Fori(0, GROUPS - 1) as g:
                with eng.Fori(0, L - 1) as l:
                    layer_body(g, l, True)
                last_body(g)
            with eng.Fori(0, L - 1) as l:
                layer_body(GROUPS - 1, l, False)
            end(GROUPS - 1)

        block = ctx.enter_context(nc.Block())

        @block.sync
        def _(sp):
            def load_x(t, s):
                sp.dma_start(x_all[:, bass.ds(t * TILE, TILE)].rearrange("p (g d) -> p g d", g=TG),
                             x_t[bass.ds(t, 1)].rearrange("t n g d -> n (t g) d")).then_inc(x_loaded[s], 16)

            def load_adj(t, s):
                sp.dma_start(adj_in[:, s].rearrange("p (g d) -> p g d", g=TG),
                             adj_t[bass.ds(t, 1)].rearrange("t n g d -> n (t g) d")).then_inc(adj_loaded[s], 16)

            load_x(0, 0)
            load_adj(0, 0)
            for s in range(1, SLOTS):
                load_x(s, s)
                load_adj(s, s)
            for s in range(SLOTS):
                sp.wait_ge(a_done, s + 1)
                sp.wait_ge(x_loaded[s], 16)
                load_x(SLOTS + s, s)
                load_adj(SLOTS + s, s)

            def store(g):
                for s in range(SLOTS):
                    sp.wait_ge(out_done, g * SLOTS + s + 1)
                    sp.dma_start(out_t[bass.ds(g * SLOTS + s, 1)].rearrange("t n g d -> n (t g) d"),
                                 x_all[:, bass.ds((g * SLOTS + s) * TILE, TILE)].rearrange(
                                     "p (g d) -> p g d", g=TG)).then_inc(stored[s], 16)

            with sp.Fori(0, GROUPS - 2) as g:
                for s in range(SLOTS):
                    sp.wait_ge(a_done, g * SLOTS + (SLOTS + s + 1))
                    sp.wait_ge(x_loaded[s], g * 16 + 32)
                    load_x(g * SLOTS + (2 * SLOTS + s), s)
                    load_adj(g * SLOTS + (2 * SLOTS + s), s)
                store(g)
            for g in range(GROUPS - 2, GROUPS):
                store(g)
            for s in range(SLOTS):
                sp.wait_ge(stored[s], 16 * GROUPS)

        @block.tensor
        def _(pe):
            def transpose(dst, src):
                for q in range(TG):
                    last = nc.tensor.transpose(graph(dst, q), graph(src, q), ident_sb[:])
                return last

            def three(ps, w_hi, w_lo, m_hi, m_lo, start, stop):
                nc.tensor.matmul(ps[:], w_hi, m_hi, start=start, stop=False)
                nc.tensor.matmul(ps[:], w_hi, m_lo, start=False, stop=False)
                return nc.tensor.matmul(ps[:], w_lo, m_hi, start=False, stop=stop)

            def h_products(K, s, first_unit=False):
                pe.wait_ge(h_lo_done, K + 1)
                if not first_unit:
                    pe.wait_ge(r_done, K)
                three(ps_r, gate(u_hi, 0), gate(u_lo, 0), h_hi[:, s], h_lo[:, s], True, False)
                if not first_unit:
                    pe.wait_ge(z_done, K)
                three(ps_z, gate(u_hi, 1), gate(u_lo, 1), h_hi[:, s], h_lo[:, s], True, False)
                if not first_unit:
                    pe.wait_ge(rhn_done, K)
                three(ps_hn, gate(u_hi, 2), gate(u_lo, 2), h_hi[:, s], h_lo[:, s], True, True)

            def s_products(K, s):
                pe.wait_ge(s_lo_done, K + 1)
                par = s % 2
                for k, (ps, ready) in enumerate(((ps_r, r_mm), (ps_z, z_mm), (ps_in, in_mm))):
                    three(ps, gate(v_cur, k), gate(v_cur, k, CG), s_hi[:, par], s_lo[:, par],
                          k == 2, True).then_inc(ready, 1)

            def aggregate(K, s):
                pe.wait_ge(nat_lo_done, K + 1)
                for q in range(TG):
                    a_q = graph(a[:, s], q)
                    nc.tensor.matmul(graph(ps_s, q), graph(nat_hi[:, s], q), a_q, start=True, stop=False)
                    last = nc.tensor.matmul(graph(ps_s, q), graph(nat_lo[:, s], q), a_q, start=False, stop=True)
                last.then_inc(s_mm, 1)

            def step(K, j, layer_starts, next_group):
                s = (j + 2) % SLOTS
                h_products(K, s)
                transpose_back(K, j, next_group)
                pe.wait_ge(s_lo_done, K + 1)
                aggregate(K + 1, (s + 1) % SLOTS)
                pe.wait_ge(n_done, K)
                if layer_starts is not None:
                    pe.wait_ge(vcur_done, layer_starts)
                s_products(K, s)

            def transpose_back(K, j, next_group):
                pe.wait_ge(h_done, K - 1)
                transpose(ps_back[j % 2], h[:, j]).then_inc(t_mm, 1)
                if next_group is not None:
                    transpose_h0(next_group, j, K + 2)

            def transpose_h0(group, j, before):
                pe.wait_ge(h0_done, group * SLOTS + j + 1)
                if before is not None:
                    pe.wait_ge(h_hi_done, before)
                transpose(ps_t0, h0[:, j * TILE:(j + 1) * TILE]).then_inc(t0_mm, 1)

            def fold(l):
                if l >= 1:
                    pe.wait_ge(v_hi_done, l)
                nc.tensor.matmul(ps_v[:, 0:CG], fold_in[:, l], wih_sb[:], start=True, stop=True).then_inc(v_mm, 1)

            def first():
                pe.wait_ge(ident_loaded, 16)
                transpose_h0(0, 0, None)
                pe.wait_ge(wih_loaded, 32)
                fold(0)
                pe.wait_ge(a_done, 1)
                aggregate(0, 0)
                pe.wait_ge(u_lo_done, 1)
                h_products(0, 0, True)
                transpose_h0(0, 1, 1)
                fold(1)
                pe.wait_ge(s_lo_done, 1)
                pe.wait_ge(a_done, 2)
                aggregate(1, 1)
                pe.wait_ge(vcur_done, 1)
                s_products(0, 0)
                fold(2)
                h_products(1, 1)
                transpose_h0(0, 2, 2)
                fold(3)
                pe.wait_ge(s_lo_done, 2)
                pe.wait_ge(a_done, 3)
                aggregate(2, 2)
                pe.wait_ge(n_done, 1)
                s_products(1, 1)
                fold(4)
                transpose_h0(0, 3, 3)

            def layer_body(g, l, more):
                K0 = pe.snap(g * UNITS + l * SLOTS + 2)
                pe.wait_ge(a_done, g * SLOTS + SLOTS)
                for j in range(SLOTS):
                    starts = g * L + l + 2 if j == 2 else None
                    step(K0 + j, j, starts, None)

            def last_body(g):
                for j in range(SLOTS):
                    K = g * UNITS + (UNITS - SLOTS + 2 + j)
                    if j:
                        pe.wait_ge(a_done, (g + 1) * SLOTS + j)
                    starts = g * L + (L + 1) if j == 2 else None
                    step(K, j, starts, g + 1)

            def end(g):
                for j in range(SLOTS):
                    K = g * UNITS + UNITS - SLOTS + 2 + j
                    if j < 2:
                        h_products(K, j + 2)
                    transpose_back(K, j, None)
                    if j == 0:
                        pe.wait_ge(s_lo_done, K + 1)
                        aggregate(K + 1, SLOTS - 1)
                    if j < 2:
                        pe.wait_ge(n_done, K)
                        s_products(K, j + 2)

            schedule(pe, first, layer_body, last_body, end)

        @block.scalar
        def _(act):
            def initial_state_high(count, s):
                act.wait_ge(h0_done, count)
                nc.scalar.activation(nat_hi[:, s], h0[:, s * TILE:(s + 1) * TILE], ACT.Relu).then_inc(nat_hi_done, 1)
                act.wait_ge(t0_mm, count)
                nc.scalar.activation(h[:, s], ps_t0[:], ACT.Relu)
                nc.scalar.activation(h_hi[:, s], ps_t0[:], ACT.Relu).then_inc(h_hi_done, 1)

            def s_high(K, par):
                act.wait_ge(s_mm, K + 1)
                nc.scalar.copy(s_hi[:, par], ps_s[:]).then_inc(s_hi_done, 1)

            def gate_r(K):
                act.wait_ge(r_mm, K + 1)
                nc.scalar.activation(r[:], ps_r[:], ACT.Sigmoid, bias=b_sum[:, 0:1]).then_inc(r_done, 1)

            def gate_z(K, par, prologue=False):
                act.wait_ge(z_mm, K + 1)
                if not prologue:
                    act.wait_ge(zdiff_done, K - 1)
                nc.scalar.activation(z[:, par], ps_z[:], ACT.Sigmoid, bias=b_sum[:, 1:2]).then_inc(z_done, 1)

            def gate_n(K, par, prologue=False):
                act.wait_ge(npre_done, K + 1)
                if not prologue:
                    act.wait_ge(h_done, K - 1)
                nc.scalar.activation(n[:, par], ps_in[:], ACT.Tanh, bias=b_ih[:, 2:3]).then_inc(n_done, 1)

            def copy_v(K, off):
                act.wait_ge(in_mm, K)
                nc.scalar.copy(v_cur[:], v_all[:, bass.ds(off, 2 * CG)]).then_inc(vcur_done, 1)

            def step(K, j, group, v_off):
                act.wait_ge(in_mm, K)
                s_high(K + 1, (j + 3) % 2)
                gate_r(K)
                gate_z(K, j % 2)
                if group is not None:
                    initial_state_high(group * SLOTS + j + 1, j)
                else:
                    act.wait_ge(t_mm, K - 1)
                    nc.scalar.copy(nat_hi[:, j], ps_back[j % 2][:]).then_inc(nat_hi_done, 1)
                    act.wait_ge(h_done, K - 1)
                    nc.scalar.copy(h_hi[:, j], h[:, j]).then_inc(h_hi_done, 1)
                if v_off is not None:
                    copy_v(K + 1, v_off)
                gate_n(K, j % 2)

            def v_high(l):
                act.wait_ge(v_mm, l + 1)
                if l:
                    act.wait_ge(v_lo_done, l)
                nc.scalar.copy(v_whole[:], ps_v[:, 0:CG])
                nc.scalar.copy(v_all[:, 2 * CG * l:2 * CG * l + CG], ps_v[:, 0:CG]).then_inc(v_hi_done, 1)

            def first():
                act.dma_start(wih_sb[:], w_ihT).then_inc(wih_loaded, 16)
                act.dma_start(fold_in[:], fold_lhs).then_inc(wih_loaded, 16)
                act.dma_start(whh_sb[:], w_hhT).then_inc(w_loaded, 16)
                act.wait_ge(consts_set, 2)
                nc.scalar.activation(table_warm[:], eps[:, 0:1], ACT.Sigmoid)
                act.wait_ge(w_loaded, 16)
                nc.scalar.copy(u_hi[:], whh_sb[:]).then_inc(u_hi_done, 1)
                initial_state_high(1, 0)
                v_high(0)
                s_high(0, 0)
                act.wait_ge(v_lo_done, 1)
                nc.scalar.copy(v_cur[:], v_all[:, 0:2 * CG]).then_inc(vcur_done, 1)
                initial_state_high(2, 1)
                v_high(1)
                s_high(1, 1)
                act.wait_ge(bias_done, 1)
                gate_r(0)
                gate_z(0, 0, True)
                v_high(2)
                initial_state_high(3, 2)
                gate_n(0, 0, True)
                v_high(3)
                s_high(2, 0)
                gate_r(1)
                gate_z(1, 1, True)
                v_high(4)
                initial_state_high(4, 3)
                gate_n(1, 1, True)

            def layer_body(g, l, more):
                K0 = act.snap(g * UNITS + l * SLOTS + 2)
                for j in range(SLOTS):
                    step(K0 + j, j, None, (l + 1) * (2 * CG) if j == 1 else None)

            def last_body(g):
                for j in range(SLOTS):
                    step(g * UNITS + (UNITS - SLOTS + 2 + j), j, g + 1, 0 if j == 1 else None)

            def end(g):
                for j in range(2):
                    K = g * UNITS + UNITS - SLOTS + 2 + j
                    if j == 0:
                        act.wait_ge(in_mm, K)
                        s_high(K + 1, (j + 3) % 2)
                    gate_r(K)
                    gate_z(K, j % 2)
                    gate_n(K, j % 2)

            schedule(act, first, layer_body, last_body, end)

        @block.vector
        def _(dve):
            def bn_stats(loaded, off, s_sem):
                dve.wait_ge(s_sem, loaded)
                for q in range(TG):
                    last = nc.vector.bn_stats(bn[:, q], x_all[:, bass.ds(off + q * P, P)])
                last.then_inc(bn_done, 1)

            def bn_aggr(par=0):
                for q in range(TG):
                    last = nc.vector.bn_aggr(mean_var[:, par, q], bn[:, q])
                last.then_inc(aggr_done, 1)

            def layernorm(count, off, h0_off, par=0):
                dve.wait_ge(rstd_done, count)
                for q in range(TG):
                    last = nc.vector.tensor_scalar(h0[:, bass.ds(h0_off + q * P, P)], x_all[:, bass.ds(off + q * P, P)],
                                                   mean_var[:, par, q, 0:1], rstd[:, par, q:q + 1], ALU.subtract, ALU.mult)
                last.then_inc(h0_done, 1)

            def adjacency(loaded, s):
                dve.wait_ge(adj_loaded[s], loaded)
                nc.vector.tensor_scalar(a[:, s], adj_in[:, s], 0.0, None, ALU.not_equal).then_inc(a_done, 1)

            def low(dst, whole, high, done):
                nc.vector.tensor_tensor(dst, whole, high, ALU.subtract).then_inc(done, 1)

            def initial_state_low(count, s):
                initial_natural_low(count, s)
                initial_transposed_low(count, s)

            def initial_transposed_low(count, s):
                dve.wait_ge(h_hi_done, count)
                low(h_lo[:, s], h[:, s], h_hi[:, s], h_lo_done)

            def initial_natural_low(count, s):
                dve.wait_ge(nat_hi_done, count)
                nc.vector.scalar_tensor_tensor(out=nat_lo[:, s], in0=h0[:, s * TILE:(s + 1) * TILE], scalar=0.0,
                                               in1=nat_hi[:, s], op0=ALU.max, op1=ALU.subtract).then_inc(nat_lo_done, 1)

            def s_low(K, par):
                dve.wait_ge(s_hi_done, K + 1)
                low(s_lo[:, par], ps_s[:], s_hi[:, par], s_lo_done)

            def new_state(K, s):
                dve.wait_ge(zdiff_done, K + 1)
                nc.vector.tensor_tensor(h[:, s], n[:, s % 2], zdiff[:], ALU.add).then_inc(h_done, 1)

            def r_times_hn(K):
                dve.wait_ge(r_done, K + 1)
                nc.vector.scalar_tensor_tensor(out=rhn[:], in0=ps_hn[:], scalar=b_hh[:, 2:3], in1=r[:],
                                               op0=ALU.add, op1=ALU.mult).then_inc(rhn_done, 1)

            def n_input(K):
                dve.wait_ge(in_mm, K + 1)
                dve.wait_ge(rhn_done, K + 1)
                nc.vector.tensor_tensor(ps_in[:], ps_in[:], rhn[:], ALU.add).then_inc(npre_done, 1)

            def final(tile, j, count):
                dve.wait_ge(t_mm, count)
                for q in range(TG):
                    x_q = x_all[:, bass.ds(tile * TILE + (j * TILE + q * P), P)]
                    last = nc.vector.scalar_tensor_tensor(
                        out=x_q, in0=graph(ps_back[j % 2], q), scalar=mask_sb[:, bass.ds(tile * TG + (j * TG + q), 1)],
                        in1=x_q, op0=ALU.mult, op1=ALU.add)
                last.then_inc(out_done, 1)

            def step(K, j, g, last_layer, bn_tiles=None):
                if bn_tiles is not None:
                    dve.wait_ge(bn_done, bn_tiles)
                s_low(K + 1, (j + 3) % 2)
                if last_layer:
                    adjacency(g * 16 + 32, j)
                r_times_hn(K)
                new_state(K - 1, (j + 1) % SLOTS)
                n_input(K)
                if last_layer:
                    initial_state_low(K + 3, j)
                    final(g * SLOTS, j, K - 1)
                else:
                    dve.wait_ge(nat_hi_done, K + 3)
                    low(nat_lo[:, j], ps_back[j % 2][:], nat_hi[:, j], nat_lo_done)
                    dve.wait_ge(h_hi_done, K + 3)
                    low(h_lo[:, j], h[:, j], h_hi[:, j], h_lo_done)

            def first():
                def moments(s):
                    if s:
                        dve.wait_ge(aggr_done, s)
                    bn_stats(16, s * TILE, x_loaded[s])
                    dve.wait_ge(bn_done, s + 1)
                    bn_aggr(s % 2)

                def tile_inputs(s):
                    layernorm(s + 1, s * TILE, s * TILE, s % 2)
                    adjacency(16, s)

                moments(0)
                tile_inputs(0)
                moments(1)
                dve.wait_ge(u_hi_done, 1)
                low(u_lo[:], whh_sb[:], u_hi[:], u_lo_done)
                initial_state_low(1, 0)
                tile_inputs(1)
                s_low(0, 0)
                dve.wait_ge(misc_loaded, 48)
                nc.vector.tensor_tensor(b_sum[:], b_ih[:], b_hh[:], ALU.add).then_inc(bias_done, 1)
                initial_state_low(2, 1)
                moments(2)
                s_low(1, 1)
                r_times_hn(0)
                moments(3)
                tile_inputs(2)
                n_input(0)
                initial_natural_low(3, 2)
                tile_inputs(3)
                initial_transposed_low(3, 2)
                s_low(2, 0)
                r_times_hn(1)
                new_state(0, 0)
                n_input(1)
                initial_state_low(4, 3)

            def layer_body(g, l, more):
                K0 = dve.snap(g * UNITS + l * SLOTS + 2)
                ln_tile = g * SLOTS + l + SLOTS
                if more:
                    ln_off = dve.snap(ln_tile * TILE)
                for j in range(SLOTS):
                    step(K0 + j, j, None, False, ln_tile + 1 if more and j == 1 else None)
                    if more and j == 0:
                        for s in range(1, SLOTS):
                            dve.wait_ge(x_loaded[s], g * 16 + 32)
                        bn_stats(g * 16 + 32, ln_off, x_loaded[0])
                    if more and j == 1:
                        bn_aggr()
                    if more and j == 3:
                        layernorm(ln_tile + 1, ln_off, l * TILE)

            def last_body(g):
                for j in range(SLOTS):
                    step(g * UNITS + (UNITS - SLOTS + 2 + j), j, g, True)

            def end(g):
                for j in range(SLOTS):
                    K = g * UNITS + UNITS - SLOTS + 2 + j
                    final(g * SLOTS, j, K - 1)
                    if j == 0:
                        s_low(K + 1, (j + 3) % 2)
                    if j < 2:
                        r_times_hn(K)
                    if j < 2:
                        new_state(K - 1, (j + 1) % SLOTS)
                        n_input(K)
                    if j == 2:
                        dve.wait_ge(n_done, K)
                        nc.vector.tensor_tensor(diff[:], h[:, 3], n[:, 1], ALU.subtract).then_inc(diff_done, 1)
                        dve.wait_ge(diff_done, K)
                        nc.vector.tensor_tensor(zdiff[:], z[:, 1], diff[:], ALU.mult).then_inc(zdiff_done, 1)
                        new_state(K - 1, 3)

            schedule(dve, first, layer_body, last_body, end)

        @block.gpsimd
        def _(pool):
            def inv_std(count, par=0):
                pool.wait_ge(aggr_done, count)
                nc.gpsimd.tensor_tensor(var_eps[:, par], mean_var[:, par, :, 1], eps[:], ALU.add).then_inc(var_done, 1)
                pool.wait_ge(var_done, count)
                nc.gpsimd.tensor_tensor(rstd[:, par], var_eps[:, par], neg_half[:], ALU.pow).then_inc(rstd_done, 1)

            def unit(K, s, before=True):
                pool.wait_ge(n_done, K + 1)
                nc.gpsimd.tensor_tensor(diff[:], h[:, s], n[:, s % 2], ALU.subtract).then_inc(diff_done, 1)
                if before:
                    pool.wait_ge(h_done, K)
                pool.wait_ge(diff_done, K + 1)
                nc.gpsimd.tensor_tensor(zdiff[:], z[:, s % 2], diff[:], ALU.mult).then_inc(zdiff_done, 1)

            def v_low(l):
                pool.wait_ge(v_hi_done, l + 1)
                nc.gpsimd.tensor_tensor(v_all[:, 2 * CG * l + CG:2 * CG * (l + 1)], v_whole[:],
                                        v_all[:, 2 * CG * l:2 * CG * l + CG], ALU.subtract).then_inc(v_lo_done, 1)

            def first():
                nc.gpsimd.memset(eps[:], EPS).then_inc(consts_set, 1)
                nc.gpsimd.memset(neg_half[:], -0.5).then_inc(consts_set, 1)
                pool.dma_start(ident_sb[:], ident).then_inc(ident_loaded, 16)
                pool.dma_start(b_ih[:], bias_ih).then_inc(misc_loaded, 16)
                pool.dma_start(b_hh[:], bias_hh).then_inc(misc_loaded, 16)
                pool.dma_start(mask_sb[:], maskT).then_inc(misc_loaded, 16)
                pool.wait_ge(consts_set, 2)
                inv_std(1, 0)
                inv_std(2, 1)
                v_low(0)
                v_low(1)
                inv_std(3, 0)
                inv_std(4, 1)
                v_low(2)
                unit(0, 0, False)
                v_low(3)
                v_low(4)
                unit(1, 1)

            def layer_body(g, l, more):
                K0 = pool.snap(g * UNITS + l * SLOTS + 2)
                for j in range(SLOTS):
                    if more and j == 2:
                        inv_std(g * SLOTS + l + (SLOTS + 1))
                    unit(K0 + j, (j + 2) % SLOTS)

            def last_body(g):
                for j in range(SLOTS):
                    unit(g * UNITS + (UNITS - SLOTS + 2 + j), (j + 2) % SLOTS)

            def end(g):
                unit(g * UNITS + UNITS - 2, SLOTS - 2)

            schedule(pool, first, layer_body, last_body, end)


def kernel(x, adj, nodemask, L0_gnn_weight, L0_gnn_w_ih, L0_gnn_w_hh, L0_gnn_b_ih, L0_gnn_b_hh):
    import numpy as np
    import concourse.bacc as bacc
    from concourse.bass_utils import run_bass_kernel_spmd

    nc = bacc.Bacc("TRN2", target_bir_lowering=False, num_devices=1)
    laid_out = {
        "x": np.asarray(x),
        "adj": np.asarray(adj),
        "maskT": np.asarray(nodemask).T,
        "fold_lhs": np.asarray(L0_gnn_weight).transpose(2, 0, 1),
        "w_ihT": np.asarray(L0_gnn_w_ih).T,
        "w_hhT": np.asarray(L0_gnn_w_hh).T,
        "bias_ih": np.asarray(L0_gnn_b_ih).reshape(GATES, P).T,
        "bias_hh": np.asarray(L0_gnn_b_hh).reshape(GATES, P).T,
        "ident": np.eye(P, dtype=np.float32),
    }
    arrays, args = {}, []
    for name, a in laid_out.items():
        a = np.ascontiguousarray(a)
        arrays[f"in_{name}"] = a
        args.append(nc.dram_tensor(f"in_{name}", a.shape, mybir.dt.from_np(a.dtype), kind="ExternalInput").ap())
    out = nc.dram_tensor("out_0", np.asarray(x).shape, F32, kind="ExternalOutput").ap()
    gnn_kernel(nc, *args, out)
    r = run_bass_kernel_spmd(nc, [arrays], core_ids=[0])
    return r.results[0]["out_0"]
```
